# Optimizing a Trainium2 kernel written in Bass

```python
import numpy as np
import jax
import jax.numpy as jnp

def _softmax(x, axis=-1):
    return jax.nn.softmax(x, axis=axis)

def _gelu(x):
    return jax.nn.gelu(x, approximate=True)

def _silu(x):
    return jax.nn.silu(x)

def _sigmoid(x):
    return jax.nn.sigmoid(x)

def _layernorm(x, axis=-1, eps=1e-05):
    m = jnp.mean(x, axis=axis, keepdims=True)
    v = jnp.var(x, axis=axis, keepdims=True)
    return (x - m) / jnp.sqrt(v + eps)

def _scatter_add(tgt, idx, src, axis=0):
    return tgt.at[idx].add(src)

def _segment_sum(src, seg, n):
    return jax.ops.segment_sum(src, seg, n)
kernel_name = 'mk_dlrm_tower_d1_rec_r8_537a46'

def setup_inputs(seed: int=0):
    np.random.seed(seed)
    _w = jnp.asarray

    def _rec_inputs():
        import jax
        import jax.numpy as jnp
        _tk = jax.random.key(seed)
        dense_ctx = jax.random.normal(jax.random.fold_in(_tk, 190), (2048, 16), jnp.float32)
        ids = jnp.stack([jax.random.randint(jax.random.fold_in(_tk, 200 + f), (2048,), 0, v, jnp.int32) for f, v in enumerate([1250, 1250, 1250, 12500, 12500, 1250, 1000, 1000, 12500, 12500, 1000, 12500, 12500, 1250, 12500, 12500, 1250, 1250, 1000, 1000, 1250, 1250, 1000, 1000, 1250, 1000, 1250, 1000, 1000, 1000, 1000, 1250])], axis=1)
        tbl_0 = 0.05 * jax.random.normal(jax.random.fold_in(_tk, 500 + 0), (1250, 256), jnp.float32)
        tbl_1 = 0.05 * jax.random.normal(jax.random.fold_in(_tk, 500 + 1), (1250, 256), jnp.float32)
        tbl_2 = 0.05 * jax.random.normal(jax.random.fold_in(_tk, 500 + 2), (1250, 256), jnp.float32)
        tbl_3 = 0.05 * jax.random.normal(jax.random.fold_in(_tk, 500 + 3), (12500, 256), jnp.float32)
        tbl_4 = 0.05 * jax.random.normal(jax.random.fold_in(_tk, 500 + 4), (12500, 256), jnp.float32)
        tbl_5 = 0.05 * jax.random.normal(jax.random.fold_in(_tk, 500 + 5), (1250, 256), jnp.float32)
        tbl_6 = 0.05 * jax.random.normal(jax.random.fold_in(_tk, 500 + 6), (1000, 256), jnp.float32)
        tbl_7 = 0.05 * jax.random.normal(jax.random.fold_in(_tk, 500 + 7), (1000, 256), jnp.float32)
        tbl_8 = 0.05 * jax.random.normal(jax.random.fold_in(_tk, 500 + 8), (12500, 256), jnp.float32)
        tbl_9 = 0.05 * jax.random.normal(jax.random.fold_in(_tk, 500 + 9), (12500, 256), jnp.float32)
        tbl_10 = 0.05 * jax.random.normal(jax.random.fold_in(_tk, 500 + 10), (1000, 256), jnp.float32)
        tbl_11 = 0.05 * jax.random.normal(jax.random.fold_in(_tk, 500 + 11), (12500, 256), jnp.float32)
        tbl_12 = 0.05 * jax.random.normal(jax.random.fold_in(_tk, 500 + 12), (12500, 256), jnp.float32)
        tbl_13 = 0.05 * jax.random.normal(jax.random.fold_in(_tk, 500 + 13), (1250, 256), jnp.float32)
        tbl_14 = 0.05 * jax.random.normal(jax.random.fold_in(_tk, 500 + 14), (12500, 256), jnp.float32)
        tbl_15 = 0.05 * jax.random.normal(jax.random.fold_in(_tk, 500 + 15), (12500, 256), jnp.float32)
        tbl_16 = 0.05 * jax.random.normal(jax.random.fold_in(_tk, 500 + 16), (1250, 256), jnp.float32)
        tbl_17 = 0.05 * jax.random.normal(jax.random.fold_in(_tk, 500 + 17), (1250, 256), jnp.float32)
        tbl_18 = 0.05 * jax.random.normal(jax.random.fold_in(_tk, 500 + 18), (1000, 256), jnp.float32)
        tbl_19 = 0.05 * jax.random.normal(jax.random.fold_in(_tk, 500 + 19), (1000, 256), jnp.float32)
        tbl_20 = 0.05 * jax.random.normal(jax.random.fold_in(_tk, 500 + 20), (1250, 256), jnp.float32)
        tbl_21 = 0.05 * jax.random.normal(jax.random.fold_in(_tk, 500 + 21), (1250, 256), jnp.float32)
        tbl_22 = 0.05 * jax.random.normal(jax.random.fold_in(_tk, 500 + 22), (1000, 256), jnp.float32)
        tbl_23 = 0.05 * jax.random.normal(jax.random.fold_in(_tk, 500 + 23), (1000, 256), jnp.float32)
        tbl_24 = 0.05 * jax.random.normal(jax.random.fold_in(_tk, 500 + 24), (1250, 256), jnp.float32)
        tbl_25 = 0.05 * jax.random.normal(jax.random.fold_in(_tk, 500 + 25), (1000, 256), jnp.float32)
        tbl_26 = 0.05 * jax.random.normal(jax.random.fold_in(_tk, 500 + 26), (1250, 256), jnp.float32)
        tbl_27 = 0.05 * jax.random.normal(jax.random.fold_in(_tk, 500 + 27), (1000, 256), jnp.float32)
        tbl_28 = 0.05 * jax.random.normal(jax.random.fold_in(_tk, 500 + 28), (1000, 256), jnp.float32)
        tbl_29 = 0.05 * jax.random.normal(jax.random.fold_in(_tk, 500 + 29), (1000, 256), jnp.float32)
        tbl_30 = 0.05 * jax.random.normal(jax.random.fold_in(_tk, 500 + 30), (1000, 256), jnp.float32)
        tbl_31 = 0.05 * jax.random.normal(jax.random.fold_in(_tk, 500 + 31), (1250, 256), jnp.float32)
        _rk = jax.random.fold_in(_tk, 7)
        W_top1 = 0.0441942 * jax.random.normal(jax.random.fold_in(_tk, 801), (512, 512), jnp.float32)
        W_top2 = 0.0441942 * jax.random.normal(jax.random.fold_in(_tk, 802), (512, 256), jnp.float32)
        W_top3 = 0.0625 * jax.random.normal(jax.random.fold_in(_tk, 803), (256, 1), jnp.float32)
        b_top1 = jnp.zeros((512,), jnp.float32)
        b_top2 = jnp.zeros((256,), jnp.float32)
        return (dense_ctx, ids, tbl_0, tbl_1, tbl_2, tbl_3, tbl_4, tbl_5, tbl_6, tbl_7, tbl_8, tbl_9, tbl_10, tbl_11, tbl_12, tbl_13, tbl_14, tbl_15, tbl_16, tbl_17, tbl_18, tbl_19, tbl_20, tbl_21, tbl_22, tbl_23, tbl_24, tbl_25, tbl_26, tbl_27, tbl_28, tbl_29, tbl_30, tbl_31, W_top1, b_top1, W_top2, b_top2, W_top3)
    dense_ctx, ids, tbl_0, tbl_1, tbl_2, tbl_3, tbl_4, tbl_5, tbl_6, tbl_7, tbl_8, tbl_9, tbl_10, tbl_11, tbl_12, tbl_13, tbl_14, tbl_15, tbl_16, tbl_17, tbl_18, tbl_19, tbl_20, tbl_21, tbl_22, tbl_23, tbl_24, tbl_25, tbl_26, tbl_27, tbl_28, tbl_29, tbl_30, tbl_31, W_top1, b_top1, W_top2, b_top2, W_top3 = _rec_inputs()

    def _L0_rec_setup():
        import jax, jax.numpy as jnp
        import numpy as np
        B, N, D = (1024, 32, 256)
        key = jax.random.key(seed)
        x = jax.random.normal(key, (B, N, D), dtype=jnp.float32)
        return {'x': x}
    _L0_rec_all = _L0_rec_setup()
    _L0_rec_in = {k: v for k, v in _L0_rec_all.items() if k in ()}
    del _L0_rec_all
    return {'dense_ctx': dense_ctx, 'ids': ids, 'tbl_0': tbl_0, 'tbl_1': tbl_1, 'tbl_2': tbl_2, 'tbl_3': tbl_3, 'tbl_4': tbl_4, 'tbl_5': tbl_5, 'tbl_6': tbl_6, 'tbl_7': tbl_7, 'tbl_8': tbl_8, 'tbl_9': tbl_9, 'tbl_10': tbl_10, 'tbl_11': tbl_11, 'tbl_12': tbl_12, 'tbl_13': tbl_13, 'tbl_14': tbl_14, 'tbl_15': tbl_15, 'tbl_16': tbl_16, 'tbl_17': tbl_17, 'tbl_18': tbl_18, 'tbl_19': tbl_19, 'tbl_20': tbl_20, 'tbl_21': tbl_21, 'tbl_22': tbl_22, 'tbl_23': tbl_23, 'tbl_24': tbl_24, 'tbl_25': tbl_25, 'tbl_26': tbl_26, 'tbl_27': tbl_27, 'tbl_28': tbl_28, 'tbl_29': tbl_29, 'tbl_30': tbl_30, 'tbl_31': tbl_31, 'W_top1': W_top1, 'b_top1': b_top1, 'W_top2': W_top2, 'b_top2': b_top2, 'W_top3': W_top3}

def reference(dense_ctx, ids, tbl_0, tbl_1, tbl_2, tbl_3, tbl_4, tbl_5, tbl_6, tbl_7, tbl_8, tbl_9, tbl_10, tbl_11, tbl_12, tbl_13, tbl_14, tbl_15, tbl_16, tbl_17, tbl_18, tbl_19, tbl_20, tbl_21, tbl_22, tbl_23, tbl_24, tbl_25, tbl_26, tbl_27, tbl_28, tbl_29, tbl_30, tbl_31, W_top1, b_top1, W_top2, b_top2, W_top3):
    import jax
    import jax.numpy as jnp

    def _L0_rec_ref(x):
        import jax, jax.numpy as jnp
        import numpy as np
        B, N, D = (1024, 32, 256)
        'Second-order feature interaction (DLRM dot interaction).\n\n            Computes dot(x_i, x_j) for all field pairs i < j (self_interaction=False),\n            flattened in row-major upper-triangular order -> [B, N*(N-1)/2].\n            Matches tf.boolean_mask(dot_products, strictly_upper_mask) ordering.\n            '
        b, n, d = x.shape
        iu, ju = jnp.triu_indices(n, k=1)
        dots = jnp.einsum('bnd,bmd->bnm', x, x)
        return dots[:, iu, ju]
    e = jnp.stack([tbl_0[ids[:, 0]], tbl_1[ids[:, 1]], tbl_2[ids[:, 2]], tbl_3[ids[:, 3]], tbl_4[ids[:, 4]], tbl_5[ids[:, 5]], tbl_6[ids[:, 6]], tbl_7[ids[:, 7]], tbl_8[ids[:, 8]], tbl_9[ids[:, 9]], tbl_10[ids[:, 10]], tbl_11[ids[:, 11]], tbl_12[ids[:, 12]], tbl_13[ids[:, 13]], tbl_14[ids[:, 14]], tbl_15[ids[:, 15]], tbl_16[ids[:, 16]], tbl_17[ids[:, 17]], tbl_18[ids[:, 18]], tbl_19[ids[:, 19]], tbl_20[ids[:, 20]], tbl_21[ids[:, 21]], tbl_22[ids[:, 22]], tbl_23[ids[:, 23]], tbl_24[ids[:, 24]], tbl_25[ids[:, 25]], tbl_26[ids[:, 26]], tbl_27[ids[:, 27]], tbl_28[ids[:, 28]], tbl_29[ids[:, 29]], tbl_30[ids[:, 30]], tbl_31[ids[:, 31]]], axis=1)
    z = _L0_rec_ref(e)
    z = z.reshape(z.shape[0], -1)
    h = jnp.concatenate([z, dense_ctx], axis=1)
    h = jnp.maximum(h @ W_top1 + b_top1, 0.0)
    h = jnp.maximum(h @ W_top2 + b_top2, 0.0)
    y = h @ W_top3
    return y

_drawn_inputs = setup_inputs


def setup_inputs(seed=0):
    import zlib

    import numpy as np

    out = dict(_drawn_inputs(seed))
    spreads = {'b_top1': (0.0, 0.1), 'b_top2': (0.0, 0.1)}
    factors = {}
    for name, (base, spread) in spreads.items():
        noise = np.random.default_rng([zlib.crc32(name.encode()), seed]).standard_normal(out[name].shape)
        drawn = base * np.exp(spread * noise) if base else spread * noise
        out[name] = jnp.asarray(drawn.astype(out[name].dtype))
    for name, factor in factors.items():
        out[name] = (out[name] * factor).astype(out[name].dtype)
    return out
```

```python
from contextlib import ExitStack

import concourse.bass as bass
from concourse import mybir

F32 = mybir.dt.float32
I32 = mybir.dt.int32
ALU = mybir.AluOpType
ACT = mybir.ActivationFunctionType

P = 128
SQ = 32
FG = 4


def pick_order(n, n_dense):
    half = n // 2

    def row(a, b):
        return a * (n - 1) - a * (a - 1) // 2 + b - a - 1

    order = []
    for j in range(n - 1):
        for k in range(1, half + 1):
            order.append(row(j, j + k) if j + k < n else row(j + k - n, j + 1))
    return order + [n * (n - 1) // 2 + d for d in range(n_dense)]


def dlrm_tower(nc, dense, ids, tables, w1, b1, w2, b2, w3, out):
    B, N = ids.shape
    D = tables[0].shape[1]
    ND = dense.shape[1]
    F1, H1 = w1.shape
    H2 = w2.shape[1]
    TILES = B // P
    STEPS = TILES // 2
    DC = D // P
    NG = N // FG
    Q = P // SQ
    HALF = N // 2
    FC = F1 // P
    C1 = H1 // P
    C2 = H2 // P
    PAIR = 2 * P
    assert N == SQ and DC == 2 and ND == HALF and F1 == N * HALF and TILES % 2 == 0

    with ExitStack() as ctx:
        def sb(name, shape, dt=F32):
            return ctx.enter_context(nc.sbuf_tensor(name, shape, dt))

        def psum(name, shape):
            return ctx.enter_context(nc.psum_tensor(name, shape, F32))

        def sem(name):
            return ctx.enter_context(nc.semaphore(name))

        ids_all = sb("ids_all", [P, TILES, N], I32)
        ids_now = sb("ids_now", [P, 2, N], I32)
        rows = sb("rows", [P, 2, N, D])
        turned = sb("turned", [P, DC, P, N])
        dots = sb("dots", [P, N * N])
        picked = sb("picked", [P, 2, F1])
        feats = sb("feats", [P, FC, PAIR])
        hid1 = sb("hid1", [P, C1, PAIR])
        hid2 = sb("hid2", [P, C2, PAIR])
        y_row = sb("y_row", [1, B])
        w1_sb = sb("w1_sb", [P, FC, H1])
        w2_sb = sb("w2_sb", [P, C1, H2])
        w3_sb = sb("w3_sb", [P, C2])
        b1_sb = sb("b1_sb", [P, C1])
        b2_sb = sb("b2_sb", [P, C2])
        ident = sb("ident", [P, P])

        turn_ps = [psum(f"turn_ps{c}", [P, FG, P]) for c in range(DC)]
        dots_ps = psum("dots_ps", [P, SQ, N])
        feat_ps = psum("feat_ps", [P, FC, P])
        hid1_ps = psum("hid1_ps", [P, C1, PAIR])
        hid2_ps = psum("hid2_ps", [P, C2, PAIR])
        y_ps = feat_ps[0:1, :, :].rearrange("p c s -> p (c s)")[:, 0:PAIR]

        ids_first = sem("ids_first")
        ids_landed = sem("ids_landed")
        ids_copied = sem("ids_copied")
        weights_landed = sem("weights_landed")
        ident_zero = sem("ident_zero")
        ident_ready = sem("ident_ready")
        rows_landed = [[sem(f"rows_landed{u}_{g}") for g in range(NG)] for u in range(2)]
        turn_ready = [sem(f"turn_ready{c}") for c in range(DC)]
        turn_moved = [sem(f"turn_moved{c}") for c in range(DC)]
        dots_ready = sem("dots_ready")
        dots_moved = sem("dots_moved")
        pairs_picked = sem("pairs_picked")
        dense_landed = [sem(f"dense_landed{u}") for u in range(2)]
        feat_ready = sem("feat_ready")
        feat_moved = sem("feat_moved")
        hid1_ready = sem("hid1_ready")
        hid1_moved = sem("hid1_moved")
        hid2_ready = sem("hid2_ready")
        hid2_moved = sem("hid2_moved")
        y_ready = sem("y_ready")
        y_moved = sem("y_moved")
        y_stored = sem("y_stored")

        flat = dots[:]
        pairs = bass.AP(flat.tensor, flat.offset + 1, [list(flat.ap[0]), [N + 1, N - 1], [1, HALF]])

        block = ctx.enter_context(nc.Block())

        def steps(eng, body):
            body(0, True, False)
            with eng.Fori(1, STEPS - 1) as i:
                body(i, False, False)
            body(STEPS - 1, False, True)

        N_WEIGHTS = 5

        @block.sync
        def _(sp):
            ids_t = ids.rearrange("(t p) f -> p t f", p=P)
            sp.dma_start(ids_now[:], ids_t[:, 0:2, :]).then_inc(ids_first, 16)
            sp.dma_start(ids_all[:], ids_t).then_inc(ids_landed, 16)
            sp.dma_start(w1_sb[:], w1.rearrange("(c p) n -> p c n", p=P)).then_inc(weights_landed, 16)
            sp.dma_start(w2_sb[:], w2.rearrange("(c p) n -> p c n", p=P)).then_inc(weights_landed, 16)
            with nc.allow_non_contiguous_dma(reason="a bias column for each partition, a few hundred elements"):
                sp.dma_start(b1_sb[:], b1.rearrange("(c p) -> p c", p=P)).then_inc(weights_landed, 16)
                sp.dma_start(b2_sb[:], b2.rearrange("(c p) -> p c", p=P)).then_inc(weights_landed, 16)
                sp.dma_start(w3_sb[:], w3.rearrange("(c p) a -> p (c a)", p=P)).then_inc(weights_landed, 16)

            def body(i, first, last):
                for u in range(2):
                    if not first:
                        sp.wait_ge(feat_ready, i * 2 + (u - 1))
                    sp.dma_start(picked[:, u, F1 - ND:], dense[bass.ds(i * PAIR + u * P, P), :]).then_inc(dense_landed[u], 16)
            steps(sp, body)
            sp.wait_ge(y_moved, STEPS)
            sp.dma_start(out.rearrange("b a -> a b"), y_row[:]).then_inc(y_stored, 16)
            sp.wait_ge(y_stored, 16)

        @block.gpsimd
        def _(pool):
            pool.memset(ident[:], 0.0).then_inc(ident_zero, 1)
            pool.wait_ge(ident_zero, 1)
            pool.affine_select(out=ident[:], in_=ident[:], compare_op=ALU.not_equal, fill=1.0, base=0,
                               pattern=[[-1, P]], channel_multiplier=1).then_inc(ident_ready, 1)
            pool.wait_ge(ids_first, 16)

            def body(i, first, last):
                if not first:
                    ids_count = [pool.snap(i * 2 + (u - 1)) for u in range(2)]
                    turn_count = [pool.snap(i * (2 * NG) + (u - 1) * NG) for u in range(2)]
                    for count in ids_count + turn_count:
                        pool.compute_val(count)
                for u in range(2):
                    if not first:
                        pool.wait_ge(ids_first, 16)
                        pool.wait_ge(ids_copied, ids_count[u])
                        pool.wait_ge(turn_ready[1], turn_count[u])
                    for f in range(N):
                        pool.indirect_dma_start(
                            rows[:, u, f, :], None, tables[f],
                            bass.IndirectOffsetOnAxis(ap=ids_now[:, u, f:f + 1], axis=0),
                        ).then_inc(rows_landed[u][f // FG], 16)

            steps(pool, body)

        @block.tensor
        def _(pe):
            def turn(i, u, first):
                for g in range(NG):
                    pe.wait_ge(rows_landed[u][g], i * (16 * FG) + 16 * FG)
                    for c in range(DC):
                        if not (first and u == 0 and g == 0):
                            pe.wait_ge(turn_moved[c], i * (2 * NG) + (u * NG + g))
                        for k in range(FG):
                            last = pe.transpose(turn_ps[c][:, k, :], rows[:, u, g * FG + k, c * P:(c + 1) * P], ident[:])
                        last.then_inc(turn_ready[c], 1)

            def dot(i, u, first):
                for c in range(DC):
                    pe.wait_ge(turn_moved[c], i * (2 * NG) + (u + 1) * NG)
                if not (first and u == 0):
                    pe.wait_ge(dots_moved, i * 2 + u)
                for s in range(SQ):
                    for q in range(Q):
                        for c in range(DC):
                            x = turned[:, c, q * SQ + s, :]
                            last = pe.matmul(dots_ps[q * SQ:(q + 1) * SQ, s, :], x, x, start=(c == 0), stop=(c == DC - 1))
                last.then_inc(dots_ready, 1)

            def feature(i, u, first):
                pe.wait_ge(pairs_picked, i * 2 + (u + 1))
                pe.wait_ge(dense_landed[u], i * 16 + 16)
                if u == 1:
                    pe.wait_ge(feat_moved, i * 2 + 1)
                elif not first:
                    pe.wait_ge(y_moved, i)
                for c in range(FC):
                    last = pe.transpose(feat_ps[:, c, :], picked[:, u, c * P:(c + 1) * P], ident[:])
                last.then_inc(feat_ready, 1)

            def mlp(i, first):
                if first:
                    pe.wait_ge(weights_landed, 16 * N_WEIGHTS)
                pe.wait_ge(feat_moved, i * 2 + 2)
                for n in range(C1):
                    if not first and n % 2 == 0:
                        pe.wait_ge(hid1_moved, i * C1 + (n + 2 - C1))
                    for c in range(FC):
                        last = pe.matmul(hid1_ps[:, n, :], w1_sb[:, c, n * P:(n + 1) * P], feats[:, c, :],
                                         start=(c == 0), stop=(c == FC - 1))
                    if n % 2 == 1:
                        last.then_inc(hid1_ready, 1)
                if not first:
                    pe.wait_ge(hid2_moved, i * C2)
                for n in range(C2):
                    for c in range(C1):
                        if n == 0:
                            pe.wait_ge(hid1_moved, i * C1 + (c + 1))
                        last = pe.matmul(hid2_ps[:, n, :], w2_sb[:, c, n * P:(n + 1) * P], hid1[:, c, :],
                                         start=(c == 0), stop=(c == C1 - 1))
                last.then_inc(hid2_ready, 1)
                for c in range(C2):
                    pe.wait_ge(hid2_moved, i * C2 + (c + 1))
                    last = pe.matmul(y_ps, w3_sb[:, c:c + 1], hid2[:, c, :], start=(c == 0), stop=(c == C2 - 1))
                last.then_inc(y_ready, 1)

            pe.wait_ge(ident_ready, 1)

            def body(i, first, last):
                turn(i, 0, first)
                dot(i, 0, first)
                turn(i, 1, first)
                feature(i, 0, first)
                dot(i, 1, first)
                feature(i, 1, first)
                mlp(i, first)

            steps(pe, body)

        def move_turned(eng, copy, c, i, u, first):
            if not (first and u == 0):
                eng.wait_ge(dots_ready, i * 2 + u)
            for g in range(NG):
                eng.wait_ge(turn_ready[c], i * (2 * NG) + (u * NG + g + 1))
                copy(turned[:, c, :, g * FG:(g + 1) * FG],
                     turn_ps[c][:].rearrange("p f s -> p s f")).then_inc(turn_moved[c], 1)

        @block.vector
        def _(dve):
            def body(i, first, last):
                for u in range(2):
                    move_turned(dve, dve.tensor_copy, 0, i, u, first)
                    if not last:
                        if first and u == 0:
                            dve.wait_ge(ids_landed, 16)
                        dve.tensor_copy(ids_now[:, u, :], ids_all[:, bass.ds(i * 2 + (u + 2), 1), :].rearrange("p a f -> p (a f)")).then_inc(ids_copied, 1)
                    dve.wait_ge(dots_ready, i * 2 + (u + 1))
                    dve.transpose(dots[:].rearrange("p (j i) -> p j i", j=N),
                                  dots_ps[:].rearrange("p s j -> p j s")).then_inc(dots_moved, 1)
                    dve.wait_ge(dots_moved, i * 2 + (u + 1))
                    if not first:
                        dve.wait_ge(feat_ready, i * 2 + (u - 1))
                    dve.tensor_copy(picked[:, u, 0:F1 - ND].rearrange("p (j k) -> p j k", k=HALF),
                                    pairs).then_inc(pairs_picked, 1)
                dve.wait_ge(y_ready, i + 1)
                dve.tensor_copy(y_row[:, bass.ds(i * PAIR, PAIR)], y_ps).then_inc(y_moved, 1)

            steps(dve, body)

        @block.scalar
        def _(act):
            act.wait_ge(weights_landed, 16 * N_WEIGHTS)

            def body(i, first, last):
                for u in range(2):
                    move_turned(act, act.copy, 1, i, u, first)
                for u in range(2):
                    act.wait_ge(feat_ready, i * 2 + (u + 1))
                    act.copy(feats[:, :, u * P:(u + 1) * P], feat_ps[:]).then_inc(feat_moved, 1)
                for n in range(C1):
                    if n % 2 == 0:
                        act.wait_ge(hid1_ready, i * (C1 // 2) + (n // 2 + 1))
                    act.activation(hid1[:, n, :], hid1_ps[:, n, :], ACT.Relu, bias=b1_sb[:, n:n + 1]).then_inc(hid1_moved, 1)
                act.wait_ge(hid2_ready, i + 1)
                for n in range(C2):
                    act.activation(hid2[:, n, :], hid2_ps[:, n, :], ACT.Relu, bias=b2_sb[:, n:n + 1]).then_inc(hid2_moved, 1)

            steps(act, body)


def kernel(**inputs):
    import numpy as _np
    import concourse.bacc as _bacc
    from concourse import mybir as _mybir
    from concourse.bass_utils import run_bass_kernel_spmd as _run

    nc = _bacc.Bacc("TRN2", target_bir_lowering=False, num_devices=1)
    n_tables = sum(name.startswith("tbl_") for name in inputs)
    laid = {name: _np.ascontiguousarray(a) for name, a in inputs.items()}
    laid["W_top1"] = _np.ascontiguousarray(laid["W_top1"][pick_order(n_tables, laid["dense_ctx"].shape[1])])
    arrays = {f"in_{name}": a for name, a in laid.items()}
    arg = {
        name: nc.dram_tensor(f"in_{name}", a.shape, _mybir.dt.from_np(a.dtype), kind="ExternalInput").ap()
        for name, a in laid.items()
    }
    n_samples = laid["ids"].shape[0]
    out = nc.dram_tensor("out_0", (n_samples, 1), _mybir.dt.float32, kind="ExternalOutput").ap()
    dlrm_tower(nc, arg["dense_ctx"], arg["ids"], [arg[f"tbl_{f}"] for f in range(n_tables)],
               arg["W_top1"], arg["b_top1"], arg["W_top2"], arg["b_top2"], arg["W_top3"], out)
    r = _run(nc, [arrays], core_ids=[0])
    return r.results[0]["out_0"]
```

```python
from contextlib import ExitStack

import concourse.bass as bass
from concourse import mybir

F32 = mybir.dt.float32
BF16 = mybir.dt.bfloat16
I32 = mybir.dt.int32
ALU = mybir.AluOpType
ACT = mybir.ActivationFunctionType

P = 128
SQ = 32
FG = 4
HOTS = (2, 1)
HOT = max(HOTS)
HOT_USE = 5
PARTS = 3
RING = 3


def slot_order(table_rows):
    by_size = sorted(range(len(table_rows)), key=lambda f: (table_rows[f], -f))
    hot = sorted(by_size[:HOT])
    return hot + [f for f in range(len(table_rows)) if f not in hot]


def pick_order(fields, n_dense):
    n = len(fields)
    half = n // 2

    def row(slot_a, slot_b):
        a, b = sorted((fields[slot_a], fields[slot_b]))
        return a * (n - 1) - a * (a - 1) // 2 + b - a - 1

    order = []
    for j in range(n - 1):
        for k in range(1, half + 1):
            order.append(row(j, j + k) if j + k < n else row(j + k - n, j + 1))
    return order + [n * (n - 1) // 2 + d for d in range(n_dense)]


def dlrm_tower(nc, dense, ids, tables, fields, w1, b1, w2, b2, w3, out):
    B, N = ids.shape
    D = tables[0].shape[1]
    ND = dense.shape[1]
    F1, H1 = w1.shape
    H2 = w2.shape[1]
    TILES = B // P
    STEPS = TILES // 2
    DC = D // P
    NG = N // FG
    Q = P // SQ
    HALF = N // 2
    FC = F1 // P
    C1 = H1 // P
    C2 = H2 // P
    BLOCKS = 4
    BG = SQ // BLOCKS
    USES = NG + BLOCKS
    V = tables[fields[0]].shape[0]
    VC = -(-V // P)
    VP = V // VC
    assert USES % RING == 0 and HOT < FG and VP * VC == V
    assert all(tables[f].shape[0] == V for f in fields[:HOT])
    assert N == SQ and DC == 2 and ND == HALF and F1 == N * HALF and TILES % 2 == 0

    with ExitStack() as ctx:
        def sb(name, shape, dt=F32):
            return ctx.enter_context(nc.sbuf_tensor(name, shape, dt))

        def psum(name, shape):
            return ctx.enter_context(nc.psum_tensor(name, shape, F32))

        def sem(name):
            return ctx.enter_context(nc.semaphore(name))

        ids_all = sb("ids_all", [P, TILES, N], I32)
        ids_now = sb("ids_now", [P, 2, N], I32)
        rows = [sb(f"rows{u}", [P, N - HOTS[u], D]) for u in range(2)]
        turned = sb("turned", [P, DC, SQ, Q, N])
        blocks = sb("blocks", [P, SQ, N])
        squares = sb("squares", [P, N * N])
        picked = sb("picked", [P, 2, F1])
        feats = sb("feats", [P, FC, P])
        hid1 = sb("hid1", [P, C1, P])
        hid2 = sb("hid2", [P, C2, P])
        y_row = sb("y_row", [1, B])
        w1_sb = sb("w1_sb", [P, FC, H1])
        w2_sb = sb("w2_sb", [P, C1, H2])
        w3_sb = sb("w3_sb", [P, C2])
        b1_sb = sb("b1_sb", [P, C1])
        b2_sb = sb("b2_sb", [P, C2])
        ident = sb("ident", [P, P])
        hot_rest = sb("hot_rest", [VP, HOT, VC, D])
        hot_part = sb("hot_part", [VP, PARTS, HOT, VC, D], BF16)
        hot_ids = sb("hot_ids", [P, HOT])
        one_hot = sb("one_hot", [VP, 2, VC, HOT, P], BF16)
        row_int = sb("row_int", [VP, VC], I32)
        row_no = sb("row_no", [VP, VC])

        ring_ps = [psum(f"ring_ps{k}", [P, 2, FG, P]) for k in range(RING)]
        feat_ps = psum("feat_ps", [P, FC, P])
        hid1_ps = feat_ps
        hid2_ps = psum("hid2_ps", [P, FC, P])
        y_ps = hid2_ps[0:1, C2, :]
        ids_ps = hid2_ps[0:VP, 0:HOT, :]

        ids_first = sem("ids_first")
        ids_landed = sem("ids_landed")
        ids_copied = sem("ids_copied")
        weights_landed = sem("weights_landed")
        ident_zero = sem("ident_zero")
        ident_ready = sem("ident_ready")
        rows_landed = [[sem(f"rows_landed{u}_{g}") for g in range(NG)] for u in range(2)]
        ring_ready = sem("ring_ready")
        ring_moved = [sem("ring_moved_dve"), sem("ring_moved_act")]
        tables_landed = [sem(f"tables_landed{h}") for h in range(HOT)]
        row_ints_made = sem("row_ints_made")
        row_nos_made = sem("row_nos_made")
        parts_made_act = sem("parts_made_act")
        parts_made_dve = sem("parts_made_dve")
        hot_ids_made = sem("hot_ids_made")
        ids_turned = sem("ids_turned")
        one_hot_made = sem("one_hot_made")
        squared = sem("squared")
        pairs_picked = sem("pairs_picked")
        dense_landed = [sem(f"dense_landed{u}") for u in range(2)]
        feat_ready = sem("feat_ready")
        feat_moved = sem("feat_moved")
        hid1_ready = sem("hid1_ready")
        hid1_moved = sem("hid1_moved")
        hid2_ready = sem("hid2_ready")
        hid2_moved = sem("hid2_moved")
        y_ready = sem("y_ready")
        y_moved = sem("y_moved")
        y_stored = sem("y_stored")

        flat = squares[:]
        pairs = bass.AP(flat.tensor, flat.offset + 1, [list(flat.ap[0]), [N + 1, N - 1], [1, HALF]])

        block = ctx.enter_context(nc.Block())

        def groups(first, u):
            return [*range(1, HOT_USE + 1), 0, *range(HOT_USE + 1, NG)] if first and u == 0 else list(range(NG))

        def cold_slots(g, u):
            return range(max(g * FG, HOTS[u]), (g + 1) * FG)

        def steps(eng, body):
            body(0, True, False)
            with eng.Fori(1, STEPS - 1) as i:
                body(i, False, False)
            body(STEPS - 1, False, True)

        N_WEIGHTS = 5

        @block.sync
        def _(sp):
            ids_t = ids.rearrange("(t p) f -> p t f", p=P)
            sp.dma_start(ids_now[:], ids_t[:, 0:2, :]).then_inc(ids_first, 16)
            sp.dma_start(ids_all[:], ids_t).then_inc(ids_landed, 16)
            sp.wait_ge(rows_landed[0][1], 16 * FG)
            for h in range(HOT):
                sp.dma_start(hot_rest[:, h, :, :], tables[fields[h]].rearrange("(p c) d -> p c d", c=VC)).then_inc(tables_landed[h], 16)
            sp.wait_ge(rows_landed[0][3], 16 * FG)
            sp.dma_start(w1_sb[:], w1.rearrange("(c p) n -> p c n", p=P)).then_inc(weights_landed, 16)
            sp.dma_start(w2_sb[:], w2.rearrange("(c p) n -> p c n", p=P)).then_inc(weights_landed, 16)
            with nc.allow_non_contiguous_dma(reason="a bias column for each partition, a few hundred elements"):
                sp.dma_start(b1_sb[:], b1.rearrange("(c p) -> p c", p=P)).then_inc(weights_landed, 16)
                sp.dma_start(b2_sb[:], b2.rearrange("(c p) -> p c", p=P)).then_inc(weights_landed, 16)
                sp.dma_start(w3_sb[:], w3.rearrange("(c p) a -> p (c a)", p=P)).then_inc(weights_landed, 16)

            def body(i, first, last):
                for u in range(2):
                    if not first:
                        sp.wait_ge(feat_ready, i * 2 + (u - 1))
                    sp.dma_start(picked[:, u, F1 - ND:], dense[bass.ds(i * (2 * P) + u * P, P), :]).then_inc(dense_landed[u], 16)
            steps(sp, body)
            sp.wait_ge(y_moved, TILES)
            sp.dma_start(out.rearrange("b a -> a b"), y_row[:]).then_inc(y_stored, 16)
            sp.wait_ge(y_stored, 16)

        @block.gpsimd
        def _(pool):
            pool.memset(ident[:], 0.0).then_inc(ident_zero, 1)
            pool.wait_ge(ident_zero, 1)
            pool.affine_select(out=ident[:], in_=ident[:], compare_op=ALU.not_equal, fill=1.0, base=0,
                               pattern=[[-1, P]], channel_multiplier=1).then_inc(ident_ready, 1)
            pool.iota(row_int[:], [[1, VC]], base=0, channel_multiplier=VC).then_inc(row_ints_made, 1)
            pool.wait_ge(ids_first, 16)

            def body(i, first, last):
                if not first:
                    ids_count = [pool.snap(i * 2 + (u - 1)) for u in range(2)]
                    turn_count = [pool.snap(i * (4 * USES) + (u - 2) * (2 * USES) + 2 * NG) for u in range(2)]
                    for count in ids_count + turn_count:
                        pool.compute_val(count)
                for u in range(2):
                    if not first:
                        pool.wait_ge(ids_first, 16)
                        pool.wait_ge(ids_copied, ids_count[u])
                        pool.wait_ge(ring_ready, turn_count[u])
                    for g in groups(first, u):
                        for f in cold_slots(g, u):
                            pool.indirect_dma_start(
                                rows[u][:, f - HOTS[u], :], None, tables[fields[f]],
                                bass.IndirectOffsetOnAxis(ap=ids_now[:, u, fields[f]:fields[f] + 1], axis=0),
                            ).then_inc(rows_landed[u][g], 16)

            steps(pool, body)

        @block.tensor
        def _(pe):
            def ring_free(i, u, first, use):
                if not (first and u == 0 and use < RING):
                    for moved in ring_moved:
                        pe.wait_ge(moved, i * (2 * USES) + (u * USES + use + 1 - RING))

            def look_up(u, bank, c):
                for h in range(HOTS[u]):
                    for v in range(VC):
                        for part in range(PARTS):
                            pe.matmul(bank[:, h, :], hot_part[:, part, h, v, c * P:(c + 1) * P],
                                      one_hot[:, u, v, h, :], start=(v == 0 and part == 0),
                                      stop=(v == VC - 1 and part == PARTS - 1))

            def turn(i, u, first, use, g):
                ring_free(i, u, first, use)
                bank = [ring_ps[use % RING][:, c, :, :] for c in range(DC)]
                cold = cold_slots(g, u)
                if g == 0:
                    if first and u == 0:
                        pe.wait_ge(parts_made_act, 2 * HOT)
                        pe.wait_ge(parts_made_dve, 2 * HOT)
                    pe.wait_ge(one_hot_made, i * 2 + (u + 1))
                    for c in range(DC):
                        look_up(u, bank[c], c)
                pe.wait_ge(rows_landed[u][g], i * (16 * len(cold)) + 16 * len(cold))
                for c in range(DC):
                    for f in cold:
                        last = pe.transpose(bank[c][:, f - g * FG, :], rows[u][:, f - HOTS[u], c * P:(c + 1) * P], ident[:])
                    last.then_inc(ring_ready, 1)

            def dot(i, u, first, b):
                if b == 0:
                    for moved in ring_moved:
                        pe.wait_ge(moved, i * (2 * USES) + (u * USES + NG))
                ring_free(i, u, first, NG + b)
                for g in range(BG):
                    product = ring_ps[(NG + b) % RING][:, g // FG, g % FG, :]
                    for c in range(DC):
                        x = turned[:, c, b * BG + g, :, :].rearrange("p q f -> p (q f)")
                        last = pe.matmul(product, x, x, start=(c == 0), stop=(c == DC - 1))
                    if g % FG == FG - 1:
                        last.then_inc(ring_ready, 1)

            def turn_ids(n, slot, first_tile):
                pe.wait_ge(hot_ids_made, n + 1)
                if not isinstance(n, int) or n > 0:
                    if first_tile:
                        pe.wait_ge(one_hot_made, 1)
                    else:
                        pe.wait_ge(y_moved, n - 1)
                for h in range(HOTS[slot]):
                    last = pe.transpose(ids_ps[:, h, :], hot_ids[:, h:h + 1].to_broadcast([P, VP]), ident[:])
                last.then_inc(ids_turned, 1)

            def feature(n, v, landed, first_tile):
                pe.wait_ge(pairs_picked, n + 1)
                pe.wait_ge(dense_landed[v], landed)
                if not first_tile:
                    pe.wait_ge(hid1_moved, n * C1)
                for c in range(FC):
                    last = pe.transpose(feat_ps[:, c, :], picked[:, v, c * P:(c + 1) * P], ident[:])
                last.then_inc(feat_ready, 1)

            def layer1(n, first_tile):
                if first_tile:
                    pe.wait_ge(weights_landed, 16 * N_WEIGHTS)
                pe.wait_ge(feat_moved, n + 1)
                for m in range(C1):
                    for c in range(FC):
                        last = pe.matmul(hid1_ps[:, m, :], w1_sb[:, c, m * P:(m + 1) * P], feats[:, c, :],
                                         start=(c == 0), stop=(c == FC - 1))
                last.then_inc(hid1_ready, 1)

            def layer2(n, last=False):
                pe.wait_ge(hid1_moved, n * C1 + C1)
                if last:
                    pe.wait_ge(y_moved, n)
                else:
                    pe.wait_ge(one_hot_made, n + 2)
                for m in range(C2):
                    for c in range(C1):
                        last = pe.matmul(hid2_ps[:, m, :], w2_sb[:, c, m * P:(m + 1) * P], hid1[:, c, :],
                                         start=(c == 0), stop=(c == C1 - 1))
                last.then_inc(hid2_ready, 1)

            def layer3(n):
                pe.wait_ge(hid2_moved, n * C2 + C2)
                for c in range(C2):
                    last = pe.matmul(y_ps, w3_sb[:, c:c + 1], hid2[:, c, :], start=(c == 0), stop=(c == C2 - 1))
                last.then_inc(y_ready, 1)

            pe.wait_ge(ident_ready, 1)
            turn_ids(0, 0, True)

            def body(i, first, last):
                for u in range(2):
                    before = i * 2 + (u - 1)
                    mlp = not (first and u == 0)
                    first_mlp = first and u == 1
                    layer2_use = NG - 2 if last and u == 1 else NG - 1
                    for use, g in enumerate(groups(first, u)):
                        turn(i, u, first, use, g)
                        if mlp and use == 0:
                            feature(before, 1 - u, i * 16 + u * 16, first_mlp)
                        if mlp and use == 2:
                            layer1(before, first_mlp)
                        if mlp and use == layer2_use:
                            layer2(before)
                    dot(i, u, first, 0)
                    if mlp:
                        layer3(before)
                    dot(i, u, first, 1)
                    if not (last and u == 1):
                        turn_ids(before + 2, 1 - u, first and u == 0)
                    dot(i, u, first, 2)
                    dot(i, u, first, 3)

            steps(pe, body)
            feature(TILES - 1, 1, STEPS * 16, False)
            layer1(TILES - 1, False)
            layer2(TILES - 1, last=True)
            layer3(TILES - 1)

        def move_turned(eng, copy, c, i, u, use, g):
            eng.wait_ge(ring_ready, i * (4 * USES) + (u * 2 * USES + 2 * use + 1 + c))
            copy(turned[:, c, :, :, g * FG:(g + 1) * FG],
                 ring_ps[use % RING][:, c, :, :].rearrange("p f (q g) -> p g q f", q=Q)).then_inc(ring_moved[c], 1)

        def move_dots(eng, copy, moved, quarters, i, u, b):
            eng.wait_ge(ring_ready, i * (4 * USES) + (u * 2 * USES + 2 * (NG + b) + 2))
            for q in quarters:
                part = slice(q * SQ, (q + 1) * SQ)
                last = copy(blocks[part, b * BG:(b + 1) * BG, :],
                            ring_ps[(NG + b) % RING][part, :, :, q * N:(q + 1) * N].rearrange("p a g f -> p (a g) f"))
            last.then_inc(moved, 1)

        @block.vector
        def _(dve):
            def move_y(n):
                dve.wait_ge(y_ready, n + 1)
                dve.tensor_copy(y_row[:, bass.ds(n * P, P)], y_ps).then_inc(y_moved, 1)

            def find_ids(n, slot, copied):
                if copied:
                    dve.wait_ge(ids_copied, n - 1)
                if not isinstance(n, int) or n > 0:
                    dve.wait_ge(ids_turned, n)
                for h in range(HOTS[slot]):
                    f = fields[h]
                    last = dve.tensor_copy(hot_ids[:, h:h + 1], ids_now[:, slot, f:f + 1])
                last.then_inc(hot_ids_made, 1)

            def make_one_hot(n, slot):
                dve.wait_ge(ids_turned, n + 1)
                for v in range(VC):
                    last = dve.tensor_scalar(one_hot[:, slot, v, 0:HOTS[slot], :], ids_ps[:, 0:HOTS[slot], :], row_no[:, v:v + 1], None, ALU.is_equal)
                last.then_inc(one_hot_made, 1)

            def split(k):
                part, h = divmod(k, HOT)
                dve.wait_ge(parts_made_act, k + 1)
                dve.tensor_tensor((hot_rest[:, h], hot_part[:, 2, h])[part], hot_rest[:, h], hot_part[:, part, h],
                                  ALU.subtract).then_inc(parts_made_dve, 1)

            dve.wait_ge(row_ints_made, 1)
            dve.tensor_copy(row_no[:], row_int[:]).then_inc(row_nos_made, 1)
            dve.wait_ge(ids_first, 16)
            find_ids(0, 0, False)
            dve.wait_ge(row_nos_made, 1)
            make_one_hot(0, 0)

            def body(i, first, last):
                for u in range(2):
                    n = i * 2 + u
                    if not (last and u == 1):
                        find_ids(n + 1, 1 - u, not (first and u == 0))
                    for use, g in enumerate(groups(first, u)):
                        move_turned(dve, dve.tensor_copy, 0, i, u, use, g)
                        if first and u == 0 and 1 <= use <= 2 * HOT:
                            split(use - 1)
                    if not last:
                        if first and u == 0:
                            dve.wait_ge(ids_landed, 16)
                        dve.tensor_copy(ids_now[:, u, :], ids_all[:, bass.ds(i * 2 + (u + 2), 1), :].rearrange("p a f -> p (a f)")).then_inc(ids_copied, 1)
                    for b in range(BLOCKS):
                        move_dots(dve, dve.tensor_copy, ring_moved[0], range(0, Q // 2), i, u, b)
                        if b == 0 and not (first and u == 0):
                            move_y(i * 2 + (u - 1))
                        if b == 1 and not (last and u == 1):
                            make_one_hot(n + 1, 1 - u)
                    for moved in ring_moved:
                        dve.wait_ge(moved, i * (2 * USES) + (u + 1) * USES)
                    dve.transpose(squares[:].rearrange("p (j i) -> p j i", j=N),
                                  blocks[:].rearrange("p s j -> p j s")).then_inc(squared, 1)
                    dve.wait_ge(squared, i * 2 + (u + 1))
                    if not first:
                        dve.wait_ge(feat_ready, i * 2 + (u - 1))
                    dve.tensor_copy(picked[:, u, 0:F1 - ND].rearrange("p (j k) -> p j k", k=HALF),
                                    pairs).then_inc(pairs_picked, 1)

            steps(dve, body)
            move_y(TILES - 1)

        @block.scalar
        def _(act):
            def move_feature(n):
                act.wait_ge(feat_ready, n + 1)
                act.copy(feats[:], feat_ps[:]).then_inc(feat_moved, 1)

            def relu1(n):
                act.wait_ge(hid1_ready, n + 1)
                for m in range(C1):
                    act.activation(hid1[:, m, :], hid1_ps[:, m, :], ACT.Relu, bias=b1_sb[:, m:m + 1]).then_inc(hid1_moved, 1)

            def relu2(n):
                act.wait_ge(hid2_ready, n + 1)
                for m in range(C2):
                    act.activation(hid2[:, m, :], hid2_ps[:, m, :], ACT.Relu, bias=b2_sb[:, m:m + 1]).then_inc(hid2_moved, 1)

            def split(k):
                part, h = divmod(k, HOT)
                if part == 0:
                    act.wait_ge(tables_landed[h], 16)
                else:
                    act.wait_ge(parts_made_dve, h + 1)
                act.copy(hot_part[:, part, h], hot_rest[:, h]).then_inc(parts_made_act, 1)

            def body(i, first, last):
                for u in range(2):
                    before = i * 2 + (u - 1)
                    mlp = not (first and u == 0)
                    for use, g in enumerate(groups(first, u)):
                        move_turned(act, act.copy, 1, i, u, use, g)
                        if first and u == 0 and 1 <= use <= 2 * HOT:
                            split(use - 1)
                        if mlp and use == 0:
                            move_feature(before)
                        if mlp and use == 2:
                            relu1(before)
                        if mlp and use == (NG - 2 if last and u == 1 else NG - 1):
                            relu2(before)
                    if mlp:
                        act.wait_ge(squared, before + 1)
                    for b in range(BLOCKS):
                        move_dots(act, act.copy, ring_moved[1], range(Q // 2, Q), i, u, b)

            steps(act, body)
            move_feature(TILES - 1)
            relu1(TILES - 1)
            relu2(TILES - 1)


def kernel(**inputs):
    import numpy as _np
    import concourse.bacc as _bacc
    from concourse import mybir as _mybir
    from concourse.bass_utils import run_bass_kernel_spmd as _run

    nc = _bacc.Bacc("TRN2", target_bir_lowering=False, num_devices=1)
    n_tables = sum(name.startswith("tbl_") for name in inputs)
    laid = {name: _np.ascontiguousarray(a) for name, a in inputs.items()}
    fields = slot_order([laid[f"tbl_{f}"].shape[0] for f in range(n_tables)])
    laid["W_top1"] = _np.ascontiguousarray(laid["W_top1"][pick_order(fields, laid["dense_ctx"].shape[1])])
    arrays = {f"in_{name}": a for name, a in laid.items()}
    arg = {
        name: nc.dram_tensor(f"in_{name}", a.shape, _mybir.dt.from_np(a.dtype), kind="ExternalInput").ap()
        for name, a in laid.items()
    }
    n_samples = laid["ids"].shape[0]
    out = nc.dram_tensor("out_0", (n_samples, 1), _mybir.dt.float32, kind="ExternalOutput").ap()
    dlrm_tower(nc, arg["dense_ctx"], arg["ids"], [arg[f"tbl_{f}"] for f in range(n_tables)], fields,
               arg["W_top1"], arg["b_top1"], arg["W_top2"], arg["b_top2"], arg["W_top3"], out)
    r = _run(nc, [arrays], core_ids=[0])
    return r.results[0]["out_0"]
```

```python
from contextlib import ExitStack

import concourse.bass as bass
import numpy as np
from concourse import mybir

F32 = mybir.dt.float32
BF16 = mybir.dt.bfloat16
I32 = mybir.dt.int32
ALU = mybir.AluOpType
ACT = mybir.ActivationFunctionType

P = 128
SQ = 32
FG = 4
HOT = 2
HOTS = (2, 1)
HOTS_FIRST = (0, 2)
HOTS_LAST = (2, 0)
PARTS = 3
RING = 3


def slot_order(table_rows):
    by_size = sorted(range(len(table_rows)), key=lambda f: (table_rows[f], -f))
    hot = sorted(by_size[:HOT])
    return hot + [f for f in range(len(table_rows)) if f not in hot]


def pick_order(fields, n_dense):
    n = len(fields)
    half = n // 2

    def row(slot_a, slot_b):
        a, b = sorted((fields[slot_a], fields[slot_b]))
        return a * (n - 1) - a * (a - 1) // 2 + b - a - 1

    order = []
    for j in range(n - 1):
        for k in range(1, half + 1):
            order.append(row(j, j + k) if j + k < n else row(j + k - n, j + 1))
    return order + [n * (n - 1) // 2 + d for d in range(n_dense)]


def schedule(first, last):
    if first:
        order = "t0 t1 t2 d0 t3 t4 d1 t5 t6 d2 t7 d3"
    elif last:
        order = "t0 t1 t2 d0 t3 t4 d1 t5 d2 t6 t7 d3"
    else:
        order = "t0 t1 t2 t3 d0 t4 t5 d1 t6 t7 d2 d3"
    return [({"t": "turn", "d": "dots"}[x[0]], int(x[1:])) for x in order.split()]


def hots(first, last, u):
    return (HOTS_FIRST if first else HOTS_LAST if last else HOTS)[u]


def hots_of(tile, n_tiles):
    return hots(tile < 2, tile >= n_tiles - 2, tile % 2)


def lay_out_ids(ids, fields):
    n_samples, n = ids.shape
    n_tiles = n_samples // P
    out = np.zeros((P, n_tiles, n + HOT), np.int32)
    for t in range(n_tiles):
        hot = hots_of(t, n_tiles)
        of_tile = ids[t * P:(t + 1) * P][:, fields]
        out[:, t, :n - hot] = of_tile[:, hot:].reshape(n - hot, P).T
        out[:, t, n:] = of_tile[:, :HOT]
    return out


def first_rows(n_tiles, table_rows, fields):
    n = len(fields)
    begin = np.concatenate([[0], np.cumsum(table_rows)])
    out = np.zeros((P, n_tiles, n), np.int32)
    for t in range(n_tiles):
        hot = hots_of(t, n_tiles)
        out[:, t, :n - hot] = np.tile(begin[fields[hot:]], P).reshape(n - hot, P).T
    return out


def dlrm_tower(nc, dense, ids, starts, table, table_rows, fields, w1, b1, w2, b2, w3, out):
    TILES, N = starts.shape[1:]
    B = TILES * P
    D = table.shape[1]
    ND = dense.shape[1]
    F1, H1 = w1.shape
    H2 = w2.shape[1]
    STEPS = TILES // 2
    DC = D // P
    NG = N // FG
    Q = P // SQ
    HALF = N // 2
    FC = F1 // P
    C1 = H1 // P
    C2 = H2 // P
    BLOCKS = 4
    BG = SQ // BLOCKS
    USES = NG + BLOCKS
    V = table_rows[fields[0]]
    VC = -(-V // P)
    VP = V // VC
    assert USES % RING == 0 and HOT < FG and VP * VC == V
    assert FC == 4 and C1 == 4 and C2 == 2
    assert all(table_rows[f] == V for f in fields[:HOT])
    assert N == SQ and DC == 2 and ND == HALF and F1 == N * HALF and TILES % 2 == 0

    with ExitStack() as ctx:
        def sb(name, shape, dt=F32):
            return ctx.enter_context(nc.sbuf_tensor(name, shape, dt))

        def psum(name, shape):
            return ctx.enter_context(nc.psum_tensor(name, shape, F32))

        def sem(name):
            return ctx.enter_context(nc.semaphore(name))

        ids_all = sb("ids_all", [P, TILES, N + HOT], I32)
        starts_sb = sb("starts_sb", [P, TILES, N], I32)
        rows_all = sb("rows_all", [P, TILES, N], I32)
        rows_now = sb("rows_now", [P, 2, N], I32)
        most_gathers = [N - min(HOTS_FIRST[u], HOTS[u], HOTS_LAST[u]) for u in range(2)]
        rows = [sb(f"rows{u}", [P, most_gathers[u], D]) for u in range(2)]
        turned = sb("turned", [P, DC, P, N])
        blocks = sb("blocks", [P, SQ, N])
        squares = sb("squares", [P, N * N])
        picked = sb("picked", [P, 2, F1])
        feats = sb("feats", [P, FC, P])
        hid1 = sb("hid1", [P, C1, P])
        hid2 = sb("hid2", [P, C2, P])
        y_row = sb("y_row", [1, B])
        w1_sb = sb("w1_sb", [P, FC, H1])
        w2_sb = sb("w2_sb", [P, C1, H2])
        w3_sb = sb("w3_sb", [P, C2])
        b1_sb = sb("b1_sb", [P, C1])
        b2_sb = sb("b2_sb", [P, C2])
        ident = sb("ident", [P, P])
        hot_rest = sb("hot_rest", [VP, HOT, VC, D])
        hot_part = sb("hot_part", [VP, PARTS, HOT, VC, D], BF16)
        hot_ids = sb("hot_ids", [P, HOT])
        one_hot = sb("one_hot", [VP, 2, VC, HOT, P], BF16)
        row_int = sb("row_int", [VP, VC], I32)
        row_no = sb("row_no", [VP, VC])

        ring_ps = [psum(f"ring_ps{k}", [P, 2, FG, P]) for k in range(RING)]
        feat_ps = psum("feat_ps", [P, FC, P])
        hid1_ps = feat_ps
        hid2_ps = psum("hid2_ps", [P, FC, P])
        ids_ps = hid2_ps[0:VP, 0:HOT, :]
        y_ps = hid2_ps[0:1, C2, :]
        ring_banks = [ring_ps[k][:, b, :, :] for k in range(RING) for b in range(2)]
        last_feat_ps = ring_banks[:2]
        last_hid1_ps = ring_banks[2:2 + C1]
        last_hid2_ps = last_feat_ps

        ids_landed = [sem("first_ids_landed"), sem("ids_landed")]
        rows_known = sem("rows_known")
        rows_now_set = sem("rows_now_set")
        weights_landed = sem("weights_landed")
        ident_zero = sem("ident_zero")
        ident_ready = sem("ident_ready")
        rows_landed = [[sem(f"rows_landed{u}_{g}") for g in range(NG)] for u in range(2)]
        ring_ready = sem("ring_ready")
        ring_moved = [sem("ring_moved_dve"), sem("ring_moved_act")]
        tables_landed = [sem(f"tables_landed{h}") for h in range(HOT)]
        row_ints_made = sem("row_ints_made")
        row_nos_made = sem("row_nos_made")
        parts_made_act = sem("parts_made_act")
        parts_made_dve = sem("parts_made_dve")
        hot_ids_made = sem("hot_ids_made")
        ids_turned = sem("ids_turned")
        one_hot_made = sem("one_hot_made")
        squared = sem("squared")
        pairs_picked = [sem("pairs_picked_act"), sem("pairs_picked_dve")]
        dense_landed = [sem(f"dense_landed{u}") for u in range(2)]
        feat_ready = sem("feat_ready")
        feat_moved = sem("feat_moved")
        last_feat_moved = sem("last_feat_moved")
        hid1_ready = sem("hid1_ready")
        hid1_moved = sem("hid1_moved")
        hid2_ready = sem("hid2_ready")
        hid2_moved = sem("hid2_moved")
        y_ready = sem("y_ready")
        y_moved = sem("y_moved")
        y_stored = sem("y_stored")

        def pick(copy, u, half):
            j, end = ((0, HALF - 1), (HALF - 1, N - 1))[half]
            flat = squares[:]
            pairs = bass.AP(flat.tensor, flat.offset + (N + 1) * j + 1, [list(flat.ap[0]), [N + 1, end - j], [1, HALF]])
            return copy(picked[:, u, j * HALF:end * HALF].rearrange("p (j k) -> p j k", k=HALF), pairs)

        block = ctx.enter_context(nc.Block())

        def hots_next(last, u):
            return not last if u == 1 else hots(False, last, 1) > 0

        def gathers(w, hot):
            return range(max(w * FG - hot, 0), (w + 1) * FG - hot)

        def place_of(order, kind, n):
            return order.index((kind, n))

        def samples_done(products, hot):
            end = products * Q * (N - hot)
            return [w for w in range(NG) if w == 0 or gathers(w, hot)[0] * P < end]

        def steps(eng, body):
            body(0, True, False)
            with eng.Fori(1, STEPS - 1) as i:
                body(i, False, False)
            body(STEPS - 1, False, True)

        N_WEIGHTS = 5
        SPLIT_USES = (1, 4, 6, 7)
        MLP_USES = {"feature": 0, "layer1": 2, "layer2": 4, "layer3": 6}
        MLP_USES_LAST = {"feature": 1, "layer1": 3, "layer2": 5, "layer3": 7}
        IDS_USE = 8
        first_row = [sum(table_rows[:f]) for f in fields[:HOT]]

        @block.sync
        def _(sp):
            for tiles in (slice(0, 2), slice(2, TILES)):
                sp.dma_start(ids_all[:, tiles, :], ids[:, tiles, :]).then_inc(ids_landed[tiles.start // 2], 16)
                sp.dma_start(starts_sb[:, tiles, :], starts[:, tiles, :]).then_inc(ids_landed[tiles.start // 2], 16)
            for h in range(HOT):
                sp.wait_ge(rows_landed[0][h], 16 * FG)
                sp.dma_start(hot_rest[:, h, :, :], table[first_row[h]:first_row[h] + V, :].rearrange("(p c) d -> p c d", c=VC)).then_inc(tables_landed[h], 16)
            sp.wait_ge(rows_landed[0][4], 16 * FG)
            sp.dma_start(w1_sb[:], w1.rearrange("(c p) n -> p c n", p=P)).then_inc(weights_landed, 16)
            sp.dma_start(w2_sb[:], w2.rearrange("(c p) n -> p c n", p=P)).then_inc(weights_landed, 16)
            with nc.allow_non_contiguous_dma(reason="a bias column for each partition, a few hundred elements"):
                sp.dma_start(b1_sb[:], b1.rearrange("(c p) -> p c", p=P)).then_inc(weights_landed, 16)
                sp.dma_start(b2_sb[:], b2.rearrange("(c p) -> p c", p=P)).then_inc(weights_landed, 16)
                sp.dma_start(w3_sb[:], w3.rearrange("(c p) a -> p (c a)", p=P)).then_inc(weights_landed, 16)

            def body(i, first, last):
                for u in range(2):
                    if not first:
                        sp.wait_ge(feat_ready, i * 2 + (u - 1))
                    sp.dma_start(picked[:, u, F1 - ND:], dense[bass.ds(i * (2 * P) + u * P, P), :]).then_inc(dense_landed[u], 16)
            steps(sp, body)
            sp.wait_ge(y_moved, TILES)
            sp.dma_start(out.rearrange("b a -> a b"), y_row[:]).then_inc(y_stored, 16)
            sp.wait_ge(y_stored, 16)

        @block.gpsimd
        def _(pool):
            pool.memset(ident[:], 0.0).then_inc(ident_zero, 1)
            pool.wait_ge(ident_zero, 1)
            pool.affine_select(out=ident[:], in_=ident[:], compare_op=ALU.not_equal, fill=1.0, base=0,
                               pattern=[[-1, P]], channel_multiplier=1).then_inc(ident_ready, 1)
            pool.iota(row_int[:], [[1, VC]], base=0, channel_multiplier=VC).then_inc(row_ints_made, 1)

            def body(i, first, last):
                known = [i * 2 + (u + 1) for u in range(2)]
                turned_count = [i * (4 * USES) + (u - 2) * (2 * USES) + 2 * USES for u in range(2)]
                if not first:
                    known = [pool.snap(x) for x in known]
                    turned_count = [pool.snap(x) for x in turned_count]
                    for count in known + turned_count:
                        pool.compute_val(count)
                for u in range(2):
                    pool.wait_ge(ids_landed[0], 32)
                    pool.wait_ge(rows_now_set, known[u])
                    if not first:
                        pool.wait_ge(ring_ready, turned_count[u])
                    for kind, w in schedule(first and u == 0, last and u == 1):
                        if kind == "turn":
                            for k in gathers(w, hots(first, last, u)):
                                pool.indirect_dma_start(
                                    rows[u][:, k, :], None, table,
                                    bass.IndirectOffsetOnAxis(ap=rows_now[:, u, k:k + 1], axis=0),
                                ).then_inc(rows_landed[u][w], 16)

            steps(pool, body)

        @block.tensor
        def _(pe):
            def ring_free(i, u, first, use):
                if not (first and u == 0 and use < RING):
                    for moved in ring_moved:
                        pe.wait_ge(moved, i * (2 * USES) + (u * USES + use + 1 - RING))

            def look_up(u, hot, bank, c):
                for h in range(hot):
                    for v in range(VC):
                        for part in range(PARTS):
                            pe.matmul(bank[:, h, :], hot_part[:, part, h, v, c * P:(c + 1) * P],
                                      one_hot[:, u, v, h, :], start=(v == 0 and part == 0),
                                      stop=(v == VC - 1 and part == PARTS - 1))

            def turn(i, u, first, last, use, w):
                ring_free(i, u, first, use)
                bank = [ring_ps[use % RING][:, c, :, :] for c in range(DC)]
                hot = hots(first, last, u)
                if w == 0 and hot:
                    if first:
                        pe.wait_ge(parts_made_act, 2 * HOT)
                        pe.wait_ge(parts_made_dve, 2 * HOT)
                    pe.wait_ge(one_hot_made, i * 2 + u)
                    for c in range(DC):
                        look_up(u, hot, bank[c], c)
                n = len(gathers(w, hot))
                if first:
                    landed_before = 0
                else:
                    n_first, n_inner = len(gathers(w, HOTS_FIRST[u])), len(gathers(w, HOTS[u]))
                    landed_before = i * (16 * n_inner) + 16 * (n_first - n_inner)
                pe.wait_ge(rows_landed[u][w], landed_before + 16 * n)
                for c in range(DC):
                    for k in gathers(w, hot):
                        turned_row = pe.transpose(bank[c][:, (k + hot) % FG, :], rows[u][:, k, c * P:(c + 1) * P], ident[:])
                    turned_row.then_inc(ring_ready, 1)

            def dot(i, u, hot, order, use, b):
                waited = 0
                for g in range(BG):
                    if g % FG == 0:
                        turned_by = max(place_of(order, "turn", w) for w in samples_done(b * BG + g + FG, hot)) + 1
                        count = max(turned_by, use + 1 - RING)
                        if count > waited:
                            for moved in ring_moved:
                                pe.wait_ge(moved, i * (2 * USES) + (u * USES + count))
                        waited = count
                    product = ring_ps[use % RING][:, g // FG, g % FG, :]
                    s = (b * BG + g) * Q
                    for c in range(DC):
                        x = turned[:, c, s:s + Q, :].rearrange("p q f -> p (q f)")
                        last = pe.matmul(product, x, x, start=(c == 0), stop=(c == DC - 1))
                    if g % FG == FG - 1:
                        last.then_inc(ring_ready, 1)

            def turn_ids(n, first_tile):
                pe.wait_ge(hot_ids_made, n)
                if not first_tile:
                    pe.wait_ge(y_moved, n - 1)
                for h in range(HOT):
                    last = pe.transpose(ids_ps[:, h, :], hot_ids[:, h:h + 1].to_broadcast([P, VP]), ident[:])
                last.then_inc(ids_turned, 1)

            def feature(n, v, landed, first_tile):
                for half in pairs_picked:
                    pe.wait_ge(half, n + 1)
                pe.wait_ge(dense_landed[v], landed)
                if not first_tile:
                    pe.wait_ge(hid1_moved, n * C1)
                for c in range(FC):
                    last = pe.transpose(feat_ps[:, c, :], picked[:, v, c * P:(c + 1) * P], ident[:])
                last.then_inc(feat_ready, 1)

            def layer1(n, first_tile):
                if first_tile:
                    pe.wait_ge(weights_landed, 16 * N_WEIGHTS)
                pe.wait_ge(feat_moved, n + 1)
                for m in range(C1):
                    for c in range(FC):
                        last = pe.matmul(hid1_ps[:, m, :], w1_sb[:, c, m * P:(m + 1) * P], feats[:, c, :],
                                         start=(c == 0), stop=(c == FC - 1))
                last.then_inc(hid1_ready, 1)

            def layer2(n, ids_next=True):
                pe.wait_ge(hid1_moved, n * C1 + C1)
                if ids_next:
                    pe.wait_ge(one_hot_made, n + 1)
                else:
                    pe.wait_ge(y_moved, n)
                for m in range(C2):
                    for c in range(C1):
                        last = pe.matmul(hid2_ps[:, m, :], w2_sb[:, c, m * P:(m + 1) * P], hid1[:, c, :],
                                         start=(c == 0), stop=(c == C1 - 1))
                last.then_inc(hid2_ready, 1)

            def layer3(n):
                pe.wait_ge(hid2_moved, n * C2 + C2)
                for c in range(C2):
                    last = pe.matmul(y_ps, w3_sb[:, c:c + 1], hid2[:, c, :], start=(c == 0), stop=(c == C2 - 1))
                last.then_inc(y_ready, 1)

            def last_mlp(n):
                half = FC // 2
                pe.wait_ge(pairs_picked[0], n + 1)
                for c in range(FC):
                    if c == 1:
                        pe.wait_ge(pairs_picked[1], n + 1)
                        pe.wait_ge(dense_landed[1], STEPS * 16)
                    turned_feats = pe.transpose(last_feat_ps[c // half][:, c % half, :], picked[:, 1, c * P:(c + 1) * P], ident[:])
                    if c % half == half - 1:
                        turned_feats.then_inc(feat_ready, 1)
                for part in range(2):
                    pe.wait_ge((feat_moved, last_feat_moved)[part], (n + 1, 1)[part])
                    for m in range(C1):
                        for c in range(part * half, (part + 1) * half):
                            hid = pe.matmul(last_hid1_ps[m][:, 0, :], w1_sb[:, c, m * P:(m + 1) * P], feats[:, c, :],
                                            start=(c == 0), stop=(c == FC - 1))
                        if part:
                            hid.then_inc(hid1_ready, 1)
                for c in range(C1):
                    pe.wait_ge(hid1_moved, n * C1 + c + 1)
                    for m in range(C2):
                        hid = pe.matmul(last_hid2_ps[m][:, 0, :], w2_sb[:, c, m * P:(m + 1) * P], hid1[:, c, :],
                                        start=(c == 0), stop=(c == C1 - 1))
                        if c == C1 - 1:
                            hid.then_inc(hid2_ready, 1)
                pe.wait_ge(y_moved, n)
                layer3(n)

            pe.wait_ge(ident_ready, 1)

            def body(i, first, last):
                for u in range(2):
                    after = MLP_USES_LAST if last and u == 1 else MLP_USES
                    before = i * 2 + (u - 1)
                    mlp = not (first and u == 0)
                    first_mlp = first and u == 1
                    order = schedule(first and u == 0, last and u == 1)
                    for use, (kind, k) in enumerate(order):
                        if kind == "turn":
                            turn(i, u, first, last, use, k)
                        else:
                            dot(i, u, hots(first, last, u), order, use, k)
                        if mlp and use == after["feature"]:
                            feature(before, 1 - u, i * 16 + u * 16, first_mlp)
                        if mlp and use == after["layer1"]:
                            layer1(before, first_mlp)
                        if mlp and use == after["layer2"]:
                            layer2(before, ids_next=hots(first, last, u) > 0)
                        if mlp and use == after["layer3"]:
                            layer3(before)
                        if use == IDS_USE and hots_next(last, u):
                            turn_ids(before + 2, first and u == 0)

            steps(pe, body)
            last_mlp(TILES - 1)

        def move_turned(eng, copy, c, i, u, hot, use, w):
            eng.wait_ge(ring_ready, i * (4 * USES) + (u * 2 * USES + 2 * use + 1 + c))
            bank = ring_ps[use % RING][:, c, :, :].rearrange("p f s -> p (f s)")
            cold = N - hot
            if w == 0 and hot:
                copy(turned[:, c, :, 0:hot], bank[:, 0:hot * P].rearrange("p (f s) -> p s f", s=P))
            at, end = gathers(w, hot)[0] * P, (gathers(w, hot)[-1] + 1) * P
            shift = (w * FG - hot) * P
            while at < end:
                s, f = divmod(at, cold)
                whole = (end - at) // cold if f == 0 else 0
                if whole:
                    to = at + whole * cold
                    last = copy(turned[:, c, s:s + whole, hot:N],
                                bank[:, at - shift:to - shift].rearrange("p (s f) -> p s f", f=cold))
                else:
                    to = min(end, at + cold - f)
                    last = copy(turned[:, c, s, hot + f:hot + f + to - at], bank[:, at - shift:to - shift])
                at = to
            last.then_inc(ring_moved[c], 1)

        def move_dots(eng, copy, moved, quarters, i, u, use, b):
            eng.wait_ge(ring_ready, i * (4 * USES) + (u * 2 * USES + 2 * use + 2))
            for q in quarters:
                part = slice(q * SQ, (q + 1) * SQ)
                last = copy(blocks[part, b * BG:(b + 1) * BG, :],
                            ring_ps[use % RING][part, :, :, q * N:(q + 1) * N].rearrange("p a g f -> p (a g) f"))
            last.then_inc(moved, 1)

        @block.vector
        def _(dve):
            def move_y(n):
                dve.wait_ge(y_ready, n + 1)
                dve.tensor_copy(y_row[:, bass.ds(n * P, P)].rearrange("a (g q) -> a q g", q=Q),
                                y_ps.rearrange("a (q g) -> a q g", q=Q)).then_inc(y_moved, 1)

            def find_ids(n):
                if not isinstance(n, int) or n > 1:
                    dve.wait_ge(ids_turned, n - 1)
                dve.tensor_copy(hot_ids[:],
                                ids_all[:, bass.ds(n, 1), N:].rearrange("p a f -> p (a f)")).then_inc(hot_ids_made, 1)

            def set_rows(n, slot):
                dve.tensor_copy(rows_now[:, slot, :], rows_all[:, bass.ds(n, 1), :].rearrange("p a f -> p (a f)")).then_inc(rows_now_set, 1)

            def make_one_hot(n, slot):
                dve.wait_ge(ids_turned, n)
                for v in range(VC):
                    last = dve.tensor_scalar(one_hot[:, slot, v, :, :], ids_ps[:], row_no[:, v:v + 1], None, ALU.is_equal)
                last.then_inc(one_hot_made, 1)

            def split(k):
                part, h = divmod(k, HOT)
                dve.wait_ge(parts_made_act, k + 1)
                dve.tensor_tensor((hot_rest[:, h], hot_part[:, 2, h])[part], hot_rest[:, h], hot_part[:, part, h],
                                  ALU.subtract).then_inc(parts_made_dve, 1)

            for tiles in (slice(0, 2), slice(2, TILES)):
                dve.wait_ge(ids_landed[tiles.start // 2], 32)
                dve.tensor_tensor(rows_all[:, tiles, :], ids_all[:, tiles, 0:N], starts_sb[:, tiles, :],
                                  ALU.add).then_inc(rows_known, 1)
                if tiles.start == 0:
                    dve.wait_ge(rows_known, 1)
                    for slot in range(2):
                        set_rows(slot, slot)
            dve.wait_ge(rows_known, 2)
            dve.wait_ge(row_ints_made, 1)
            dve.tensor_copy(row_no[:], row_int[:]).then_inc(row_nos_made, 1)
            dve.wait_ge(row_nos_made, 1)

            def body(i, first, last):
                for u in range(2):
                    n = i * 2 + u
                    after = MLP_USES_LAST if last and u == 1 else MLP_USES
                    if hots_next(last, u):
                        find_ids(n + 1)
                    for use, (kind, k) in enumerate(schedule(first and u == 0, last and u == 1)):
                        if kind == "turn":
                            move_turned(dve, dve.tensor_copy, 0, i, u, hots(first, last, u), use, k)
                            if k == NG - 1 and not last:
                                set_rows(n + 2, u)
                        else:
                            move_dots(dve, dve.tensor_copy, ring_moved[0], range(0, Q // 2), i, u, use, k)
                        if first and u == 0 and use in SPLIT_USES:
                            split(SPLIT_USES.index(use))
                        if use == after["layer3"] and not (first and u == 0):
                            move_y(i * 2 + (u - 1))
                        if use == IDS_USE and hots_next(last, u):
                            make_one_hot(n + 1, 1 - u)
                    for moved in ring_moved:
                        dve.wait_ge(moved, i * (2 * USES) + (u + 1) * USES)
                    if not (first and u == 0):
                        dve.wait_ge(pairs_picked[0], i * 2 + u)
                    for rows_j in (slice(0, HALF), slice(HALF, N)):
                        dve.transpose(squares[:, rows_j.start * N:rows_j.stop * N].rearrange("p (j i) -> p j i", i=N),
                                      blocks[:, :, rows_j].rearrange("p s j -> p j s")).then_inc(squared, 1)
                    dve.wait_ge(squared, i * 4 + (2 * u + 2))
                    if not first:
                        dve.wait_ge(feat_ready, i * 2 + (u - 1))
                    pick(dve.tensor_copy, u, 1).then_inc(pairs_picked[1], 1)

            steps(dve, body)
            dve.wait_ge(feat_ready, TILES + 1)
            dve.tensor_copy(feats[:, FC // 2:, :], last_feat_ps[1][:, 0:FC // 2, :]).then_inc(last_feat_moved, 1)
            dve.wait_ge(hid2_ready, TILES + 1)
            dve.tensor_scalar(hid2[:, 1, :], last_hid2_ps[1][:, 0, :], b2_sb[:, 1:2], 0.0, ALU.add, ALU.max).then_inc(hid2_moved, 1)
            move_y(TILES - 1)

        @block.scalar
        def _(act):
            def move_feature(n):
                act.wait_ge(feat_ready, n + 1)
                act.copy(feats[:], feat_ps[:]).then_inc(feat_moved, 1)

            def relu1(n):
                act.wait_ge(hid1_ready, n + 1)
                for m in range(C1):
                    act.activation(hid1[:, m, :], hid1_ps[:, m, :], ACT.Relu, bias=b1_sb[:, m:m + 1]).then_inc(hid1_moved, 1)

            def relu2(n):
                act.wait_ge(hid2_ready, n + 1)
                for m in range(C2):
                    act.activation(hid2[:, m, :], hid2_ps[:, m, :], ACT.Relu, bias=b2_sb[:, m:m + 1]).then_inc(hid2_moved, 1)

            def split(k):
                part, h = divmod(k, HOT)
                if part == 0:
                    act.wait_ge(tables_landed[h], 16)
                else:
                    act.wait_ge(parts_made_dve, h + 1)
                act.copy(hot_part[:, part, h], hot_rest[:, h]).then_inc(parts_made_act, 1)

            def body(i, first, last):
                for u in range(2):
                    after = MLP_USES_LAST if last and u == 1 else MLP_USES
                    before = i * 2 + (u - 1)
                    mlp = not (first and u == 0)
                    for use, (kind, k) in enumerate(schedule(first and u == 0, last and u == 1)):
                        if kind == "turn":
                            move_turned(act, act.copy, 1, i, u, hots(first, last, u), use, k)
                        else:
                            if k == 0 and mlp:
                                act.wait_ge(squared, i * 4 + 2 * u)
                            move_dots(act, act.copy, ring_moved[1], range(Q // 2, Q), i, u, use, k)
                        if first and u == 0 and use in SPLIT_USES:
                            split(SPLIT_USES.index(use))
                        if mlp and use == after["feature"]:
                            move_feature(before)
                        if mlp and use == after["layer1"]:
                            relu1(before)
                        if mlp and use == after["layer2"]:
                            relu2(before)
                    act.wait_ge(squared, i * 4 + (2 * u + 1))
                    if not first:
                        act.wait_ge(feat_ready, i * 2 + (u - 1))
                    pick(act.copy, u, 0).then_inc(pairs_picked[0], 1)

            steps(act, body)
            act.wait_ge(feat_ready, TILES)
            act.copy(feats[:, 0:FC // 2, :], last_feat_ps[0][:, 0:FC // 2, :]).then_inc(feat_moved, 1)
            for m in range(C1):
                act.wait_ge(hid1_ready, TILES + m)
                act.activation(hid1[:, m, :], last_hid1_ps[m][:, 0, :], ACT.Relu, bias=b1_sb[:, m:m + 1]).then_inc(hid1_moved, 1)
            act.wait_ge(hid2_ready, TILES)
            act.activation(hid2[:, 0, :], last_hid2_ps[0][:, 0, :], ACT.Relu, bias=b2_sb[:, 0:1]).then_inc(hid2_moved, 1)


def kernel(**inputs):
    import numpy as _np
    import concourse.bacc as _bacc
    from concourse import mybir as _mybir
    from concourse.bass_utils import run_bass_kernel_spmd as _run

    nc = _bacc.Bacc("TRN2", target_bir_lowering=False, num_devices=1)
    n_tables = sum(name.startswith("tbl_") for name in inputs)
    laid = {name: _np.ascontiguousarray(a) for name, a in inputs.items()}
    tables = [laid.pop(f"tbl_{f}") for f in range(n_tables)]
    table_rows = [a.shape[0] for a in tables]
    fields = slot_order(table_rows)
    laid["table"] = _np.concatenate(tables, axis=0)
    laid["ids"] = _np.ascontiguousarray(lay_out_ids(laid["ids"], fields))
    laid["starts"] = _np.ascontiguousarray(first_rows(laid["ids"].shape[1], table_rows, fields))
    n_samples, n_dense = laid["dense_ctx"].shape
    laid["dense_ctx"] = _np.ascontiguousarray(
        laid["dense_ctx"].reshape(n_samples // P, SQ, P // SQ, n_dense).transpose(0, 2, 1, 3).reshape(n_samples, n_dense))
    laid["W_top1"] = _np.ascontiguousarray(laid["W_top1"][pick_order(fields, n_dense)])
    arrays = {f"in_{name}": a for name, a in laid.items()}
    arg = {
        name: nc.dram_tensor(f"in_{name}", a.shape, _mybir.dt.from_np(a.dtype), kind="ExternalInput").ap()
        for name, a in laid.items()
    }
    out = nc.dram_tensor("out_0", (n_samples, 1), _mybir.dt.float32, kind="ExternalOutput").ap()
    dlrm_tower(nc, arg["dense_ctx"], arg["ids"], arg["starts"], arg["table"], table_rows, fields,
               arg["W_top1"], arg["b_top1"], arg["W_top2"], arg["b_top2"], arg["W_top3"], out)
    r = _run(nc, [arrays], core_ids=[0])
    return r.results[0]["out_0"]
```
